# Optimizing a Trainium2 kernel written in Bass

```python
import numpy as np
import jax
import jax.numpy as jnp

def _softmax(x, axis=-1):
    return jax.nn.softmax(x, axis=axis)

def _gelu(x):
    return jax.nn.gelu(x, approximate=True)

def _silu(x):
    return jax.nn.silu(x)

def _sigmoid(x):
    return jax.nn.sigmoid(x)

def _layernorm(x, axis=-1, eps=1e-05):
    m = jnp.mean(x, axis=axis, keepdims=True)
    v = jnp.var(x, axis=axis, keepdims=True)
    return (x - m) / jnp.sqrt(v + eps)

def _scatter_add(tgt, idx, src, axis=0):
    return tgt.at[idx].add(src)

def _segment_sum(src, seg, n):
    return jax.ops.segment_sum(src, seg, n)
kernel_name = 'mk_cond_seq_d1_seqx_r2_d9a2a7'

def setup_inputs(seed: int=0):
    np.random.seed(seed)
    _w = jnp.asarray

    def _rec_inputs():
        import jax
        import jax.numpy as jnp
        _rk = jax.random.key(seed)
        x = -0.000125 + 0.9999 * jax.random.normal(jax.random.fold_in(_rk, 1), (4, 1024, 512), jnp.float32)
        _lenS = 1024 - jax.random.randint(jax.random.fold_in(_rk, 7), (4,), 0, max(1, 1024 // 4) + 1, jnp.int32)
        _lenS2 = 1024 - jax.random.randint(jax.random.fold_in(_rk, 8), (4,), 0, max(1, 1024 // 4) + 1, jnp.int32)
        cond_256 = 0.0061147 + 1.02565 * jax.random.normal(jax.random.fold_in(_rk, 11), (4, 128), jnp.float32)
        return (x, cond_256)
    x, cond_256 = _rec_inputs()

    def _L0_cond_setup():
        import jax, jax.numpy as jnp
        import numpy as np
        DIM = 512
        BN = 128
        H = 128
        DELTA_SCALE = 0.1
        key = jax.random.key(seed)
        ks = jax.random.split(key, 10)
        B, L = (16, 1024)

        def init(k, shape, fan_in):
            bound = 1.0 / np.sqrt(fan_in)
            return jax.random.uniform(k, shape, jnp.float32, -bound, bound)
        return {'x': jax.random.normal(ks[0], (B, L, DIM), jnp.float32), 'h_lang': jax.random.normal(ks[1], (B, H), jnp.float32), 'Wd': init(ks[2], (BN, DIM), DIM), 'bd': init(ks[3], (BN,), DIM), 'Wu': init(ks[4], (DIM, BN), BN), 'bu': init(ks[5], (DIM,), BN), 'Wdd': init(ks[6], (BN * DIM, H), H), 'bdd': init(ks[7], (BN * DIM,), H), 'Wdu': init(ks[8], (DIM * BN, H), H), 'bdu': init(ks[9], (DIM * BN,), H)}
    _L0_cond_all = _L0_cond_setup()
    _L0_cond_in = {k: v for k, v in _L0_cond_all.items() if k in ('Wd', 'bd', 'Wu', 'bu', 'Wdd', 'bdd', 'Wdu', 'bdu')}
    del _L0_cond_all
    return {'x': x, 'cond_256': cond_256, 'L0_cond_Wd': _L0_cond_in['Wd'], 'L0_cond_bd': _L0_cond_in['bd'], 'L0_cond_Wu': _L0_cond_in['Wu'], 'L0_cond_bu': _L0_cond_in['bu'], 'L0_cond_Wdd': _L0_cond_in['Wdd'], 'L0_cond_bdd': _L0_cond_in['bdd'], 'L0_cond_Wdu': _L0_cond_in['Wdu'], 'L0_cond_bdu': _L0_cond_in['bdu']}

def reference(x, cond_256, L0_cond_Wd, L0_cond_bd, L0_cond_Wu, L0_cond_bu, L0_cond_Wdd, L0_cond_bdd, L0_cond_Wdu, L0_cond_bdu):
    import jax
    import jax.numpy as jnp

    def _L0_cond_ref(x, h_lang, Wd, bd, Wu, bu, Wdd, bdd, Wdu, bdu):
        import jax, jax.numpy as jnp
        import numpy as np
        DIM = 512
        BN = 128
        H = 128
        DELTA_SCALE = 0.1
        B, L, D = x.shape
        dWd = ((h_lang @ Wdd.T + bdd) * DELTA_SCALE).reshape(B, BN, D)
        dWu = ((h_lang @ Wdu.T + bdu) * DELTA_SCALE).reshape(B, D, BN)
        Wd_b = Wd + dWd
        Wu_b = Wu + dWu
        down = jax.nn.relu(jnp.einsum('bld,bnd->bln', x, Wd_b) + bd)
        up = jnp.einsum('bln,bdn->bld', down, Wu_b) + bu
        return x + up
    x = _L0_cond_ref(x, cond_256, L0_cond_Wd, L0_cond_bd, L0_cond_Wu, L0_cond_bu, L0_cond_Wdd, L0_cond_bdd, L0_cond_Wdu, L0_cond_bdu)
    return x

_drawn_inputs = setup_inputs


def setup_inputs(seed=0):
    import zlib

    import numpy as np

    out = dict(_drawn_inputs(seed))
    spreads = {}
    factors = {'L0_cond_bd': 4.991}
    for name, (base, spread) in spreads.items():
        noise = np.random.default_rng([zlib.crc32(name.encode()), seed]).standard_normal(out[name].shape)
        drawn = base * np.exp(spread * noise) if base else spread * noise
        out[name] = jnp.asarray(drawn.astype(out[name].dtype))
    for name, factor in factors.items():
        out[name] = (out[name] * factor).astype(out[name].dtype)
    return out
```

```python
from contextlib import ExitStack

import concourse.bass as bass
from concourse import mybir

P = 128
QUAD = 32
B, L, D, N, H = 4, 1024, 512, 128, 128
DELTA_SCALE = 0.1

K = 16
CHUNK_ROWS = P * K
R = H // QUAD
Q = P // QUAD
COLS = K * QUAD
SLOTS = 4
CHUNKS = D * N // CHUNK_ROWS
GROUPS = CHUNKS // SLOTS
GROUP_CHUNKS_LOOPED = 2 * SLOTS
TURNS = CHUNKS // GROUP_CHUNKS_LOOPED
SQ = SLOTS * Q
PART = SQ * B
FILL = SLOTS * P + SQ * B
FILL_STEP = P + Q * B
W_RING = 4

C = D // P
I = L // P
UNIT_I = 4
DOWN_UNITS = B * I // UNIT_I
X_BANKS = DOWN_UNITS * C
HALF = D // 2
UP_I = 2
UP_UNITS = B * I // UP_I
UP_RING = 4

DOWN_AT = {2 * j + 3: j for j in range(DOWN_UNITS)}
UP_START = 19
UP_AT_A = {}
UP_AT_B = {}
_v = 0
for _t in range(UP_START, CHUNKS):
    if _t % 4 == 2 and _v < UP_UNITS:
        UP_AT_A[_t] = _v
        _v += 1
    if _v < UP_UNITS:
        UP_AT_B[_t] = _v
        _v += 1
assert _v == UP_UNITS
UP_LAG = 2
BU_START = 4
BU_PIECES = B * I
X_LOAD_AT = {-3: 0, 1: 1, 5: 2, 9: 3}


def later(count, back):
    return not isinstance(count, int) or count >= back


def hyper_adapter(nc, x, cond, Wd, bd, Wu, bu, Wdd, bdd, Wdu, bdu, out):
    fp32, fp32r = mybir.dt.float32, mybir.dt.float32r
    ALU = mybir.AluOpType
    ACT = mybir.ActivationFunctionType

    wdd_chunks = Wdd.rearrange("(c p k) h -> c p (k h)", p=P, k=K)
    wdu_chunks = Wdu.rearrange("(c p k) h -> c p (k h)", p=P, k=K)
    x_rows = x.rearrange("b (p i) d -> b p i d", p=P)
    out_rows = out.rearrange("b (p i) d -> b p i d", p=P)

    ctx = ExitStack()
    with ctx:
        def sb(name, shape, dt=fp32):
            return ctx.enter_context(nc.sbuf_tensor(name, shape, dt))

        def pb(name, shape, dt=fp32):
            return ctx.enter_context(nc.psum_tensor(name, shape, dt))

        def sem(name):
            return ctx.enter_context(nc.semaphore(name))

        xs = sb("xs", [P, B, I, D])
        w = sb("w", [P, W_RING, K * H])
        tA = sb("tA", [P, 2, 2, COLS])
        tB = sb("tB", [P, 2, 2, COLS])
        hiA = sb("hiA", [P, 2, COLS], fp32r)
        loA = sb("loA", [P, 2, COLS], fp32r)
        hiB = sb("hiB", [P, 2, 2, COLS], fp32r)
        loB = sb("loB", [P, 2, 2, COLS], fp32r)
        g_rows = sb("g_rows", [P, 2, COLS])
        wd_b = sb("wd_b", [P, C, B, N])
        wu_b = sb("wu_b", [P, B, D])
        down = sb("down", [P, B, I, P])
        xt = sb("xt", [P, 2, C, UNIT_I * P])
        base_d = sb("base_d", [P, C, N])
        base_u = sb("base_u", [P, D])
        st_full = sb("st_full", [P, 2, FILL])
        st_split = sb("st_split", [P, R - 1, FILL], fp32r)
        ident = sb("ident", [P, P])
        bu_all = sb("bu_all", [P, D])
        bd_col = sb("bd_col", [P, 1])
        h32 = sb("h32", [P, R, B])
        h_hi = sb("h_hi", [P, R, B], fp32r)
        h_lo = sb("h_lo", [P, R, B], fp32r)
        cond_rep = xt[0:B, 0, 0, :].rearrange("b (r q i) -> b r q i", q=Q, i=QUAD)
        nat = [down[:, b, 0:C, :] for b in range(B)]
        wd_nat, bdd_nat, wu_nat, bdu_nat = nat

        acc = [pb(f"acc{n}", [P, COLS]) for n in range(2)]
        gt = pb("gt", [P, C, P])
        xb = [pb(f"xb{n}", [P, UNIT_I * P]) for n in range(2)]
        dn = pb("dn", [P, UNIT_I * P])
        up = [pb(f"up{n}", [P, UP_I * HALF]) for n in range(2)] + xb

        cond_loaded = sem("cond_loaded")
        base_loaded = sem("base_loaded")
        w_loaded = [sem(f"w_loaded{n}") for n in range(W_RING)]
        x_loaded = [sem(f"x_loaded{b}") for b in range(B)]
        ident_zeroed = sem("ident_zeroed")
        ident_ready = sem("ident_ready")
        stationaries_zeroed = sem("stationaries_zeroed")
        cond_turned = sem("cond_turned")
        h_copied = sem("h_copied")
        stationaries_ready = sem("stationaries_ready")
        base_summed = sem("base_summed")
        base_turned = sem("base_turned")
        base_ready = sem("base_ready")
        tA_ready = sem("tA_ready")
        tB_ready = sem("tB_ready")
        hiA_ready = sem("hiA_ready")
        hiB_ready = sem("hiB_ready")
        loA_ready = sem("loA_ready")
        loB_ready = sem("loB_ready")
        sumA_done = sem("sumA_done")
        sumB_done = sem("sumB_done")
        g_ready = sem("g_ready")
        g_turned = sem("g_turned")
        part1_added = sem("part1_added")
        group_added = sem("group_added")
        x_turned = sem("x_turned")
        x_copied = sem("x_copied")
        down_summed = sem("down_summed")
        down_ready = sem("down_ready")
        bu_added = sem("bu_added")
        up_summed = sem("up_summed")
        unit_final = sem("unit_final")
        out_stored = sem("out_stored")

        block = ctx.enter_context(nc.Block())

        def quarter(r):
            return r % 2

        @block.sync
        def _(sp):
            def load_chunk(c, chunk, slot):
                if later(c, W_RING):
                    sp.wait_ge(tB_ready, c - W_RING + 1)
                sp.dma_start(w[:, slot, :], chunk).then_inc(w_loaded[slot], 16)

            def load_x(b):
                sp.dma_start(xs[:, b], x_rows[b]).then_inc(x_loaded[b], 16)

            def turn(it):
                for u in range(GROUP_CHUNKS_LOOPED):
                    c = GROUP_CHUNKS_LOOPED * it + u
                    load_chunk(c, wdd_chunks[c], u % W_RING)

            turn(0)
            with sp.Fori(1, TURNS) as it:
                turn(it)

            def store(v, units):
                half, b, i0 = v // UP_UNITS, v % UP_UNITS // (I // UP_I), v % (I // UP_I) * UP_I
                i0 -= (units - 1) * UP_I
                sp.wait_ge(unit_final, v + 1)
                sp.dma_start(out_rows[b, :, i0:i0 + units * UP_I, half * HALF:(half + 1) * HALF],
                             xs[:, b, i0:i0 + units * UP_I, half * HALF:(half + 1) * HALF]
                             ).then_inc(out_stored, 16)

            load_x(X_LOAD_AT[-3])
            stores = 0
            at = {t: v for d in (UP_AT_A, UP_AT_B) for t, v in d.items() if v % 4 == 3}
            for t in range(CHUNKS):
                if t in X_LOAD_AT:
                    load_x(X_LOAD_AT[t])
                load_chunk(CHUNKS + t, wdu_chunks[t], t % W_RING)
                if t - UP_LAG - W_RING - 1 in at:
                    store(at.pop(t - UP_LAG - W_RING - 1), 4)
                    stores += 1
            for t in sorted(at):
                store(at[t], 4)
                stores += 1
            for v in range(UP_UNITS + 1, 2 * UP_UNITS, 2):
                store(v, 2)
                stores += 1
            sp.wait_ge(out_stored, 16 * stores)

        @block.vector
        def _(dve):
            dve.wait_ge(cond_turned, 1)
            nc.vector.tensor_copy(h32[:], gt[:, 0, 0:R * B].rearrange("p (r b) -> p r b", b=B)
                                  ).then_inc(h_copied, 1)
            dve.wait_ge(h_copied, 1)
            nc.vector.tensor_copy(h_hi[:], h32[:]).then_inc(h_copied, 1)
            dve.wait_ge(h_copied, 2)
            nc.vector.tensor_tensor(h_lo[:], h32[:], h_hi[:].bitcast(fp32), ALU.subtract
                                    ).then_inc(h_copied, 1)
            dve.wait_ge(h_copied, 3)
            dve.wait_ge(stationaries_zeroed, 2)
            for q in range(Q):
                rows = slice(QUAD * q, QUAD * (q + 1))

                def place(st, part, q=q, rows=rows):
                    at = part * PART + q * B
                    v = st[rows].rearrange("p r (s z) -> p r s z", z=FILL_STEP)
                    return v[:, :, :, at:at + B]

                def spread(h, r0, r1, rows=rows):
                    return h[rows, r0:r1].unsqueeze(2).to_broadcast([QUAD, r1 - r0, SLOTS, B])

                nc.vector.tensor_copy(place(st_full, 0), spread(h32, 0, 2)
                                      ).then_inc(stationaries_ready, 1)
                nc.vector.tensor_copy(place(st_split, 0), spread(h_hi, 1, R)
                                      ).then_inc(stationaries_ready, 1)
                nc.vector.tensor_copy(place(st_split, 1), spread(h_lo, 1, R)
                                      ).then_inc(stationaries_ready, 1)

            def transpose_chunk(c, slot, loaded):
                chunk = w[:, slot, :].rearrange("p (k r h) -> p k r h", r=R, h=QUAD)
                dve.wait_ge(w_loaded[slot], loaded)
                if later(c, 2):
                    dve.wait_ge(sumA_done, c - 1)
                nc.vector.transpose(tA[:, slot % 2].rearrange("p r (k j) -> p k r j", j=QUAD),
                                    chunk[:, :, 0:2, :]).then_inc(tA_ready, 1)
                if later(c, 2):
                    dve.wait_ge(loB_ready, c - 1)
                nc.vector.transpose(tB[:, slot % 2].rearrange("p r (k j) -> p k r j", j=QUAD),
                                    chunk[:, :, 2:4, :]).then_inc(tB_ready, 1)

            def add_group(g, parts, base, total):
                dve.wait_ge(g_turned, g + 1)
                nc.vector.tensor_tensor(total, parts[1], base, ALU.add).then_inc(part1_added, 1)
                dve.wait_ge(part1_added, g + 1)
                nc.vector.tensor_tensor(total, parts[0], total, ALU.add).then_inc(group_added, 1)

            def turned_parts():
                v = gt[:].rearrange("p c (a s b) -> p c a s b", s=SQ, b=B)
                return [v[:, :, a] for a in range(2)]

            def add_down_group(g):
                n = bass.ds(g * SQ, SQ)
                total = wd_b[:, :, :, n].rearrange("p c b s -> p c s b")
                base = base_d[:, :, n].unsqueeze(3).to_broadcast([P, C, SQ, B])
                add_group(g, turned_parts(), base, total)

            def add_up_group(g):
                d = slice((g - GROUPS) * D // GROUPS, (g - GROUPS + 1) * D // GROUPS)
                total = wu_b[:, :, d].rearrange("p b (s c) -> p c s b", c=C)
                base = base_u[:, d].rearrange("p (s c) -> p c s", c=C)
                add_group(g, turned_parts(), base.unsqueeze(3).to_broadcast([P, C, SQ, B]), total)

            def turn(it):
                for u in range(GROUP_CHUNKS_LOOPED):
                    c = GROUP_CHUNKS_LOOPED * it + u
                    transpose_chunk(c, u % W_RING, 16 * (2 * it + u // W_RING + 1))
                    if u == 1 and isinstance(it, int):
                        dve.wait_ge(base_loaded, 16 * 6)
                        nc.vector.scalar_tensor_tensor(wd_nat, bdd_nat, DELTA_SCALE, wd_nat,
                                                       ALU.mult, ALU.add).then_inc(base_summed, 1)
                        nc.vector.scalar_tensor_tensor(wu_nat, bdu_nat, DELTA_SCALE, wu_nat,
                                                       ALU.mult, ALU.add).then_inc(base_summed, 1)
                    if u == 2 and not isinstance(it, int):
                        add_down_group(2 * it - 1)
                    if u == SLOTS + 2:
                        if isinstance(it, int):
                            dve.wait_ge(base_ready, 2)
                        add_down_group(2 * it)

            turn(0)
            with dve.Fori(1, TURNS) as it:
                turn(it)

            def finish_unit(v):
                half, b, i0 = v // UP_UNITS, v % UP_UNITS // (I // UP_I), v % (I // UP_I) * UP_I
                place = xs[:, b, i0:i0 + UP_I, half * HALF:(half + 1) * HALF]
                dve.wait_ge(bu_added, I * (b + 1))
                dve.wait_ge(up_summed, v + 1)
                nc.vector.tensor_tensor(place, up[v % UP_RING][:].rearrange("p (i d) -> p i d", d=HALF),
                                        place, ALU.add).then_inc(unit_final, 1)

            for t in range(CHUNKS):
                c = CHUNKS + t
                transpose_chunk(c, t % W_RING, 16 * (c // W_RING + 1))
                dve.wait_ge(hiA_ready, t + 1)
                nc.vector.tensor_tensor(loA[:, t % 2], tA[:, t % 2, 1], hiA[:, t % 2].bitcast(fp32),
                                        ALU.subtract).then_inc(loA_ready, 1)
                if t % SLOTS == 2:
                    g = c // SLOTS - 1
                    add_down_group(g) if g < GROUPS else add_up_group(g)
                for at in (UP_AT_A, UP_AT_B):
                    if t - UP_LAG in at:
                        finish_unit(at[t - UP_LAG])
            for t in range(CHUNKS, CHUNKS + UP_LAG):
                for at in (UP_AT_A, UP_AT_B):
                    if t - UP_LAG in at:
                        finish_unit(at[t - UP_LAG])
            add_up_group(2 * GROUPS - 1)
            for v in range(UP_UNITS, 2 * UP_UNITS):
                finish_unit(v)

        @block.scalar
        def _(act):
            for q in range(Q):
                act.dma_start(cond_rep[:, :, q, :], cond.rearrange("b (r i) -> b r i", i=QUAD)
                              ).then_inc(cond_loaded, 16)
            act.dma_start(wd_nat, Wd.rearrange("n (c d) -> n c d", c=C)).then_inc(base_loaded, 16)
            act.dma_start(bdd_nat, bdd.rearrange("(n c d) -> n c d", c=C, d=P)).then_inc(base_loaded, 16)
            act.dma_start(wu_nat, Wu.rearrange("(c d) n -> d c n", c=C)).then_inc(base_loaded, 16)
            act.dma_start(bdu_nat, bdu.rearrange("(c d n) -> d c n", c=C, n=N)).then_inc(base_loaded, 16)
            act.dma_start(bu_all[:], bu.rearrange("(o d) -> o d", o=1).to_broadcast([P, D])
                          ).then_inc(base_loaded, 16)
            act.dma_start(bd_col[:], bd.rearrange("(p o) -> p o", o=1)).then_inc(base_loaded, 16)

            def round_b(c, slot):
                act.wait_ge(tB_ready, c + 1)
                if later(c, 2):
                    act.wait_ge(sumB_done, c - 1)
                nc.scalar.activation(hiB[:, slot % 2], tB[:, slot % 2], ACT.Copy).then_inc(hiB_ready, 1)

            def copy_group(g, n):
                act.wait_ge(sumB_done, SLOTS * (g + 1))
                if later(g, 2):
                    act.wait_ge(g_turned, g - 1)
                nc.scalar.activation(g_rows[:, n].rearrange("p (j k) -> p j k", k=K),
                                     acc[n][:].rearrange("p (k j) -> p j k", k=K),
                                     ACT.Copy, scale=DELTA_SCALE).then_inc(g_ready, 1)

            def turn(it):
                for u in range(GROUP_CHUNKS_LOOPED):
                    round_b(GROUP_CHUNKS_LOOPED * it + u, u)
                    if u == 1 and not isinstance(it, int):
                        copy_group(2 * it - 1, 1)
                    if u == 2 and isinstance(it, int):
                        act.wait_ge(base_turned, 1)
                        nc.scalar.activation(base_d[:], xb[0][:].rearrange("p (c n) -> p c n", c=C),
                                             ACT.Copy).then_inc(base_ready, 1)
                        act.wait_ge(base_turned, 2)
                        nc.scalar.activation(base_u[:], xb[1][:], ACT.Copy).then_inc(base_ready, 1)
                    if u == SLOTS + 1:
                        copy_group(2 * it, 0)

            turn(0)
            with act.Fori(1, TURNS) as it:
                turn(it)

            def copy_x(m):
                j, c = m // C, m % C
                act.wait_ge(x_turned, m + 1)
                if j >= 2:
                    act.wait_ge(down_summed, j - 1)
                nc.scalar.activation(xt[:, j % 2, c, :], xb[m % 2][:], ACT.Copy).then_inc(x_copied, 1)

            def copy_down(j):
                act.wait_ge(down_summed, j + 1)
                b, i0 = j // 2, j % 2 * UNIT_I
                nc.scalar.activation(down[:, b, i0:i0 + UNIT_I, :],
                                     dn[:].rearrange("p (i l) -> p i l", i=UNIT_I),
                                     ACT.Relu, bias=bd_col[:]).then_inc(down_ready, 1)

            for t in range(CHUNKS):
                c = CHUNKS + t
                act.wait_ge(tA_ready, c + 1)
                act.wait_ge(sumA_done, c - 1)
                nc.scalar.activation(hiA[:, t % 2], tA[:, t % 2, 1], ACT.Copy).then_inc(hiA_ready, 1)
                if 1 <= t <= X_BANKS // 2:
                    copy_x(2 * (t - 1))
                round_b(c, t)
                if 1 <= t <= X_BANKS // 2:
                    copy_x(2 * (t - 1) + 1)
                if t - 1 in DOWN_AT:
                    copy_down(DOWN_AT[t - 1])
                if t % SLOTS == 1:
                    g = c // SLOTS - 1
                    copy_group(g, g % 2)
            copy_group(2 * GROUPS - 1, 1)

        @block.gpsimd
        def _(pool):
            nc.gpsimd.memset(ident[:], 0.0).then_inc(ident_zeroed, 1)
            pool.wait_ge(ident_zeroed, 1)
            nc.gpsimd.affine_select(out=ident[:], in_=ident[:], compare_op=ALU.not_equal, fill=1.0,
                                    base=0, pattern=[[-1, P]], channel_multiplier=1
                                    ).then_inc(ident_ready, 1)
            nc.gpsimd.memset(st_full[:], 0.0).then_inc(stationaries_zeroed, 1)
            nc.gpsimd.memset(st_split[:].bitcast(fp32), 0.0).then_inc(stationaries_zeroed, 1)

            def rest_b(c, slot):
                pool.wait_ge(hiB_ready, c + 1)
                nc.gpsimd.tensor_tensor(loB[:, slot % 2], tB[:, slot % 2], hiB[:, slot % 2].bitcast(fp32),
                                        ALU.subtract).then_inc(loB_ready, 1)

            def turn(it):
                for u in range(GROUP_CHUNKS_LOOPED):
                    rest_b(GROUP_CHUNKS_LOOPED * it + u, u)

            turn(0)
            with pool.Fori(1, TURNS) as it:
                turn(it)
            for t in range(CHUNKS):
                rest_b(CHUNKS + t, t)
                for piece in range(2 * (t - BU_START), 2 * (t - BU_START) + 2):
                    if 0 <= piece < BU_PIECES:
                        b, i = piece // I, piece % I
                        pool.wait_ge(x_turned, C * (piece // UNIT_I + 1))
                        nc.gpsimd.tensor_tensor(xs[:, b, i], xs[:, b, i], bu_all[:], ALU.add
                                                ).then_inc(bu_added, 1)

        @block.tensor
        def _(pe):
            pe.wait_ge(cond_loaded, 16 * Q)
            pe.wait_ge(ident_ready, 1)
            for r in range(R):
                last = nc.tensor.transpose(gt[:, 0, r * B:(r + 1) * B],
                                           cond_rep[:, r].rearrange("b q i -> b (q i)"), ident[0:B, 0:B])
            last.then_inc(cond_turned, 1)

            def stationary(st, r, s):
                return st[:, r, s * P:(s + 1) * P]

            def add_full(a, moving, r, s, start, stop):
                return nc.tensor.matmul(a, stationary(st_full, r, s), moving, start=start, stop=stop)

            def add_split(a, moving, r, s, stop=False):
                return nc.tensor.matmul(a, stationary(st_split, r - 1, s), moving, start=False, stop=stop)

            def sum_b(c, u, a):
                s = u % SLOTS
                pe.wait_ge(hiB_ready, c + 1)
                add_split(a, hiB[:, u % 2, 0], 2, s)
                add_split(a, hiB[:, u % 2, 1], 3, s)
                pe.wait_ge(loB_ready, c + 1)
                add_split(a, loB[:, u % 2, 0], 2, s)
                add_split(a, loB[:, u % 2, 1], 3, s, stop=s == SLOTS - 1).then_inc(sumB_done, 1)

            def turn_group(g, n):
                pe.wait_ge(g_ready, g + 1)
                if later(g, 1):
                    pe.wait_ge(group_added, g)
                for k in range(C):
                    last = nc.tensor.transpose(gt[:, k], g_rows[:, n, k * P:(k + 1) * P], ident[:])
                last.then_inc(g_turned, 1)

            pe.wait_ge(stationaries_ready, 3 * Q)

            def turn(it):
                for u in range(GROUP_CHUNKS_LOOPED):
                    c, s, n = GROUP_CHUNKS_LOOPED * it + u, u % SLOTS, u // SLOTS
                    if s == 0 and later(it, 1):
                        pe.wait_ge(g_ready, 2 * it + n - 1)
                    pe.wait_ge(tA_ready, c + 1)
                    add_full(acc[n][:], tA[:, u % 2, 0], 0, s, s == 0, False)
                    add_full(acc[n][:], tA[:, u % 2, 1], 1, s, False, False).then_inc(sumA_done, 1)
                    sum_b(c, u, acc[n][:])
                    if u == 1 and isinstance(it, int):
                        for k, (b, nat_w) in enumerate(((xb[0], wd_nat), (xb[1], wu_nat))):
                            pe.wait_ge(base_summed, k + 1)
                            for cc in range(C):
                                last = nc.tensor.transpose(b[:, cc * P:(cc + 1) * P], nat_w[:, cc], ident[:])
                            last.then_inc(base_turned, 1)
                    if u == 1 and not isinstance(it, int):
                        turn_group(2 * it - 1, 1)
                    if u == SLOTS + 1:
                        turn_group(2 * it, 0)

            turn(0)
            with pe.Fori(1, TURNS) as it:
                turn(it)

            def turn_x(m):
                j, c = m // C, m % C
                b, i0 = j // 2, j % 2 * UNIT_I
                pe.wait_ge(x_loaded[b], 16)
                if m >= 2:
                    pe.wait_ge(x_copied, m - 1)
                for i in range(UNIT_I):
                    last = nc.tensor.transpose(xb[m % 2][:, i * P:(i + 1) * P],
                                               xs[:, b, i0 + i, c * P:(c + 1) * P], ident[:])
                last.then_inc(x_turned, 1)

            def down_unit(j):
                pe.wait_ge(group_added, GROUPS)
                pe.wait_ge(x_copied, C * (j + 1))
                if j >= 1:
                    pe.wait_ge(down_ready, j)
                for c in range(C):
                    last = nc.tensor.matmul(dn[:], wd_b[:, c, j // 2], xt[:, j % 2, c],
                                            start=c == 0, stop=c == C - 1)
                last.then_inc(down_summed, 1)

            def up_unit(v):
                half, b, i0 = v // UP_UNITS, v % UP_UNITS // (I // UP_I), v % (I // UP_I) * UP_I
                pe.wait_ge(group_added, GROUPS + (half + 1) * GROUPS // 2)
                pe.wait_ge(down_ready, 2 * b + i0 // UNIT_I + 1)
                if v == 0:
                    pe.wait_ge(x_copied, X_BANKS)
                if v >= UP_RING:
                    pe.wait_ge(unit_final, v - UP_RING + 1)
                for i in range(UP_I):
                    last = nc.tensor.matmul(up[v % UP_RING][:, i * HALF:(i + 1) * HALF],
                                            down[:, b, i0 + i], wu_b[:, b, half * HALF:(half + 1) * HALF],
                                            start=True, stop=True)
                last.then_inc(up_summed, 1)

            for t in range(CHUNKS):
                c, s, n = CHUNKS + t, t % SLOTS, t // SLOTS % 2
                if s == 0:
                    pe.wait_ge(g_ready, c // SLOTS - 1)
                pe.wait_ge(tA_ready, c + 1)
                add_full(acc[n][:], tA[:, t % 2, 0], 0, s, s == 0, False)
                pe.wait_ge(hiA_ready, t + 1)
                add_split(acc[n][:], hiA[:, t % 2], 1, s)
                pe.wait_ge(loA_ready, t + 1)
                add_split(acc[n][:], loA[:, t % 2], 1, s).then_inc(sumA_done, 1)
                if t < X_BANKS // 2:
                    turn_x(2 * t)
                if t in UP_AT_A:
                    up_unit(UP_AT_A[t])
                sum_b(c, t, acc[n][:])
                if t < X_BANKS // 2:
                    turn_x(2 * t + 1)
                if s == 1:
                    g = c // SLOTS - 1
                    turn_group(g, g % 2)
                if t in DOWN_AT:
                    down_unit(DOWN_AT[t])
                if t in UP_AT_B:
                    up_unit(UP_AT_B[t])
            turn_group(2 * GROUPS - 1, 1)
            for v in range(UP_UNITS, 2 * UP_UNITS):
                up_unit(v)


_INS = ['x', 'cond_256', 'L0_cond_Wd', 'L0_cond_bd', 'L0_cond_Wu', 'L0_cond_bu',
        'L0_cond_Wdd', 'L0_cond_bdd', 'L0_cond_Wdu', 'L0_cond_bdu']
_OUTS = [((B, L, D), 'float32')]


def kernel(**inputs):
    import numpy as _np
    import concourse.bacc as _bacc
    from concourse import mybir as _mybir
    from concourse.bass_utils import run_bass_kernel_spmd as _run

    nc = _bacc.Bacc("TRN2", target_bir_lowering=False, num_devices=1)
    arrays, args = {}, []
    for name in _INS:
        a = _np.ascontiguousarray(inputs[name])
        arrays[f"in_{name}_dram"] = a
        args.append(nc.dram_tensor(f"in_{name}_dram", a.shape, _mybir.dt.from_np(a.dtype), kind="ExternalInput").ap())
    for i, (shape, dtype) in enumerate(_OUTS):
        dt = _mybir.dt.from_np(_np.dtype(dtype))
        args.append(nc.dram_tensor(f"out_{i}_dram", shape, dt, kind="ExternalOutput").ap())
    hyper_adapter(nc, *args)
    r = _run(nc, [arrays], core_ids=[0])
    return r.results[0]["out_0_dram"]
```

```python
from contextlib import ExitStack

import concourse.bass as bass
from concourse import mybir

P = 128
QUAD = 32
B, L, D, N, H = 4, 1024, 512, 128, 128
DELTA_SCALE = 0.1

K = 16
CHUNK_ROWS = P * K
R = H // QUAD
Q = P // QUAD
COLS = K * QUAD
SLOTS = 4
CHUNKS = D * N // CHUNK_ROWS
GROUPS = CHUNKS // SLOTS
GROUP_CHUNKS_LOOPED = 2 * SLOTS
TURNS = CHUNKS // GROUP_CHUNKS_LOOPED
SQ = SLOTS * Q
PART = SQ * B
FILL = SLOTS * P + SQ * B
FILL_STEP = P + Q * B
W_RING = 4

C = D // P
I = L // P
UNIT_I = 2
DOWN_UNITS = B * I // UNIT_I
BATCH_UNITS = I // UNIT_I
BANK_C = 2
BANK_RING = 4
X_BANKS = DOWN_UNITS * C // BANK_C
HALF = D // 2
UP_I = 2
UP_UNITS = B * I // UP_I

X_LAG = 2
XT_RING = 3
DOWN_AT = {j + 3: j for j in range(DOWN_UNITS)}
UP_START = 19
UP_AT_A = {}
UP_AT_B = {}
_v = 0
for _t in range(UP_START, CHUNKS):
    if _t % 4 == 2 and _v < UP_UNITS:
        UP_AT_A[_t] = _v
        _v += 1
    if _v < UP_UNITS:
        UP_AT_B[_t] = _v
        _v += 1
assert _v == UP_UNITS
UP_LAG = 2
BU_PIECES = B * I
BU_AT = [2 + 3 * piece // 4 for piece in range(BU_PIECES)]
X_PIECES = 2 * B
X_LOAD_AT = {0: 0, **{2 * h + 1: h for h in range(1, X_PIECES)}}
FULL_FROM = 20


def later(count, back):
    return not isinstance(count, int) or count >= back


def hyper_adapter(nc, x, cond, Wd, bd, Wu, bu, Wdd, bdd, Wdu, bdu, out):
    fp32, fp32r = mybir.dt.float32, mybir.dt.float32r
    ALU = mybir.AluOpType
    ACT = mybir.ActivationFunctionType

    wdd_chunks = Wdd.rearrange("(c p k) h -> c p (k h)", p=P, k=K)
    wdu_chunks = Wdu.rearrange("(c p k) h -> c p (k h)", p=P, k=K)
    x_rows = x.rearrange("b (p i) d -> b p i d", p=P)
    out_rows = out.rearrange("b (p i) d -> b p i d", p=P)

    ctx = ExitStack()
    with ctx:
        def sb(name, shape, dt=fp32):
            return ctx.enter_context(nc.sbuf_tensor(name, shape, dt))

        def pb(name, shape, dt=fp32):
            return ctx.enter_context(nc.psum_tensor(name, shape, dt))

        def sem(name):
            return ctx.enter_context(nc.semaphore(name))

        xs = sb("xs", [P, B, I, D])
        w = sb("w", [P, W_RING, K * H])
        tA = sb("tA", [P, 2, 2, COLS])
        tB = sb("tB", [P, 2, 2, COLS])
        hiA = sb("hiA", [P, 2, 2, COLS], fp32r)
        loA = sb("loA", [P, 2, 2, COLS], fp32r)
        hiB = sb("hiB", [P, 2, 2, COLS], fp32r)
        loB = sb("loB", [P, 2, 2, COLS], fp32r)
        g_rows = sb("g_rows", [P, 2, COLS])
        wd_b = sb("wd_b", [P, C, B, N])
        wu_b = sb("wu_b", [P, B, D])
        down = sb("down", [P, B, I, P])
        xt = sb("xt", [P, XT_RING, C, UNIT_I * P])
        base_u = sb("base_u", [P, D])
        st_split = sb("st_split", [P, R, FILL], fp32r)
        ident = sb("ident", [P, P])
        bu_all = sb("bu_all", [P, D])
        bd_col = sb("bd_col", [P, 1])
        h32 = sb("h32", [P, R, B])
        h_hi = sb("h_hi", [P, R, B], fp32r)
        h_lo = sb("h_lo", [P, R, B], fp32r)
        cond_rows = xt[0:B, 0, 0, 0:H].rearrange("b (r i) -> b r i", i=QUAD)
        cond_rep = xt[0:B, 0, 1:3, :].rearrange("b c (r q i) -> b (c r) q i", q=Q, i=QUAD)
        st_full = xs[:, B - 1, 0:3, :].rearrange("p i d -> p (i d)")[:, 0:2 * FILL].rearrange(
            "p (r z) -> p r z", z=FILL)
        base_d = xs[:, B - 1, 3, :].rearrange("p (c n) -> p c n", c=C)
        st_full2 = wd_b[:].rearrange("p c b n -> p (c b n)")[:, 0:2 * FILL].rearrange(
            "p (r z) -> p r z", z=FILL)
        nat = [down[:, b, 0:C, :] for b in range(B)]
        wd_nat, bdd_nat, wu_nat, bdu_nat = nat

        acc = [pb(f"acc{n}", [P, COLS]) for n in range(2)]
        gt = pb("gt", [P, C, P])
        dn = pb("dn", [P, UNIT_I * P])
        bank = [pb(f"bank{n}", [P, UP_I * HALF]) for n in range(BANK_RING)]

        cond_loaded = sem("cond_loaded")
        base_loaded = sem("base_loaded")
        w_loaded = [sem(f"w_loaded{n}") for n in range(W_RING)]
        x_loaded = [sem(f"x_loaded{h}") for h in range(X_PIECES)]
        ident_zeroed = sem("ident_zeroed")
        ident_ready = sem("ident_ready")
        stationaries_zeroed = sem("stationaries_zeroed")
        cond_spread = sem("cond_spread")
        cond_turned = sem("cond_turned")
        h_copied = sem("h_copied")
        full_ready = sem("full_ready")
        split_ready = sem("split_ready")
        base_summed = sem("base_summed")
        base_turned = sem("base_turned")
        base_ready = sem("base_ready")
        tA_ready = sem("tA_ready")
        tB_ready = sem("tB_ready")
        hiA_ready = sem("hiA_ready")
        hiB_ready = sem("hiB_ready")
        loA_ready = sem("loA_ready")
        loB_ready = sem("loB_ready")
        sumA_done = sem("sumA_done")
        sumB_done = sem("sumB_done")
        g_ready = sem("g_ready")
        g_turned = sem("g_turned")
        part1_added = sem("part1_added")
        group_added = sem("group_added")
        x_turned = sem("x_turned")
        x_copied = sem("x_copied")
        down_summed = sem("down_summed")
        down_ready = sem("down_ready")
        bu_added = sem("bu_added")
        up_summed = sem("up_summed")
        unit_final = sem("unit_final")
        out_stored = sem("out_stored")

        block = ctx.enter_context(nc.Block())

        def place(st, part, q):
            v = st[QUAD * q:QUAD * (q + 1)].rearrange("p r (s z) -> p r s z", z=FILL_STEP)
            return v[:, :, :, part * PART + q * B:part * PART + (q + 1) * B]

        def spread(h, q, quarters):
            rows = h[QUAD * q:QUAD * (q + 1), 0:quarters]
            return rows.unsqueeze(2).to_broadcast([QUAD, quarters, SLOTS, B])

        @block.sync
        def _(sp):
            def load_chunk(c, chunk, slot):
                if later(c, W_RING):
                    sp.wait_ge(tA_ready, c - W_RING + 1)
                sp.dma_start(w[:, slot, :], chunk).then_inc(w_loaded[slot], 16)

            def load_x(h):
                i = slice(h % 2 * I // 2, (h % 2 + 1) * I // 2)
                sp.dma_start(xs[:, h // 2, i], x_rows[h // 2, :, i]).then_inc(x_loaded[h], 16)

            def turn(it):
                for u in range(GROUP_CHUNKS_LOOPED):
                    c = GROUP_CHUNKS_LOOPED * it + u
                    load_chunk(c, wdd_chunks[c], u % W_RING)
                    if u == 1 and isinstance(it, int):
                        load_base()

            def load_base():
                sp.dma_start(wd_nat, Wd.rearrange("n (c d) -> n c d", c=C)).then_inc(base_loaded, 16)
                sp.dma_start(bdd_nat, bdd.rearrange("(n c d) -> n c d", c=C, d=P)).then_inc(base_loaded, 16)
                sp.dma_start(wu_nat, Wu.rearrange("(c d) n -> d c n", c=C)).then_inc(base_loaded, 16)
                sp.dma_start(bdu_nat, bdu.rearrange("(c d n) -> d c n", c=C, n=N)).then_inc(base_loaded, 16)
                sp.dma_start(bu_all[:], bu.rearrange("(o d) -> o d", o=1).to_broadcast([P, D])
                             ).then_inc(base_loaded, 16)
                sp.dma_start(bd_col[:], bd.rearrange("(p o) -> p o", o=1)).then_inc(base_loaded, 16)

            sp.dma_start(cond_rows, cond.rearrange("b (r i) -> b r i", i=QUAD)).then_inc(cond_loaded, 16)
            turn(0)
            with sp.Fori(1, TURNS) as it:
                turn(it)

            def store(v, units):
                half, b, i0 = v // UP_UNITS, v % UP_UNITS // (I // UP_I), v % (I // UP_I) * UP_I
                i0 -= (units - 1) * UP_I
                sp.wait_ge(unit_final, v + 1)
                sp.dma_start(out_rows[b, :, i0:i0 + units * UP_I, half * HALF:(half + 1) * HALF],
                             xs[:, b, i0:i0 + units * UP_I, half * HALF:(half + 1) * HALF]
                             ).then_inc(out_stored, 16)

            stores = 0
            at = {t: v for d in (UP_AT_A, UP_AT_B) for t, v in d.items() if v % 4 == 3}
            for t in range(CHUNKS):
                if t in X_LOAD_AT:
                    load_x(X_LOAD_AT[t])
                load_chunk(CHUNKS + t, wdu_chunks[t], t % W_RING)
                if t - UP_LAG - W_RING - 1 in at:
                    store(at.pop(t - UP_LAG - W_RING - 1), 4)
                    stores += 1
            for t in sorted(at):
                store(at[t], 4)
                stores += 1
            for v in range(UP_UNITS + 1, 2 * UP_UNITS, 2):
                store(v, 2)
                stores += 1
            sp.wait_ge(out_stored, 16 * stores)

        @block.vector
        def _(dve):
            dve.wait_ge(cond_loaded, 16)
            nc.vector.tensor_copy(cond_rep, cond_rows.unsqueeze(2).to_broadcast([B, R, Q, QUAD])
                                  ).then_inc(cond_spread, 1)
            dve.wait_ge(cond_turned, 1)
            nc.vector.tensor_copy(h32[:], gt[:, 0, 0:R * B].rearrange("p (r b) -> p r b", b=B)
                                  ).then_inc(h_copied, 1)
            dve.wait_ge(h_copied, 1)
            nc.vector.tensor_copy(h_hi[:], h32[:]).then_inc(h_copied, 1)
            dve.wait_ge(h_copied, 2)
            nc.vector.tensor_tensor(h_lo[:], h32[:], h_hi[:].bitcast(fp32), ALU.subtract
                                    ).then_inc(h_copied, 1)
            dve.wait_ge(h_copied, 3)
            dve.wait_ge(stationaries_zeroed, 1)
            for q in range(Q):
                nc.vector.tensor_copy(place(st_full, 0, q), spread(h32, q, 2)).then_inc(full_ready, 1)

            def quarters(slot, r):
                chunk = w[:, slot, :].rearrange("p (k r h) -> p k r h", r=R, h=QUAD)
                return chunk[:, :, r:r + 2, :]

            def transpose_b(c, slot, loaded):
                dve.wait_ge(w_loaded[slot], loaded)
                if later(c, 2):
                    dve.wait_ge(loB_ready, c - 1)
                nc.vector.transpose(tB[:, slot % 2].rearrange("p r (k j) -> p k r j", j=QUAD),
                                    quarters(slot, 2)).then_inc(tB_ready, 1)

            def transpose_a(c, slot):
                if later(c, 2):
                    dve.wait_ge(sumA_done, c - 1)
                nc.vector.transpose(tA[:, slot % 2].rearrange("p r (k j) -> p k r j", j=QUAD),
                                    quarters(slot, 0)).then_inc(tA_ready, 1)

            def add_group(g, parts, base, total):
                dve.wait_ge(g_turned, g + 1)
                nc.vector.tensor_tensor(total, parts[1], base, ALU.add).then_inc(part1_added, 1)
                dve.wait_ge(part1_added, g + 1)
                nc.vector.tensor_tensor(total, parts[0], total, ALU.add).then_inc(group_added, 1)

            def turned_parts():
                v = gt[:].rearrange("p c (a s b) -> p c a s b", s=SQ, b=B)
                return [v[:, :, a] for a in range(2)]

            def add_down_group(g):
                n = bass.ds(g * SQ, SQ)
                total = wd_b[:, :, :, n].rearrange("p c b s -> p c s b")
                base = base_d[:, :, n].unsqueeze(3).to_broadcast([P, C, SQ, B])
                add_group(g, turned_parts(), base, total)

            def add_up_group(g):
                d = slice((g - GROUPS) * D // GROUPS, (g - GROUPS + 1) * D // GROUPS)
                total = wu_b[:, :, d].rearrange("p b (s c) -> p c s b", c=C)
                base = base_u[:, d].rearrange("p (s c) -> p c s", c=C)
                add_group(g, turned_parts(), base.unsqueeze(3).to_broadcast([P, C, SQ, B]), total)

            def turn(it):
                for u in range(GROUP_CHUNKS_LOOPED):
                    c = GROUP_CHUNKS_LOOPED * it + u
                    transpose_b(c, u % W_RING, 16 * (2 * it + u // W_RING + 1))
                    transpose_a(c, u % W_RING)
                    if u == 3 and isinstance(it, int):
                        dve.wait_ge(base_loaded, 16 * 6)
                        nc.vector.scalar_tensor_tensor(wd_nat, bdd_nat, DELTA_SCALE, wd_nat,
                                                       ALU.mult, ALU.add).then_inc(base_summed, 1)
                        nc.vector.scalar_tensor_tensor(wu_nat, bdu_nat, DELTA_SCALE, wu_nat,
                                                       ALU.mult, ALU.add).then_inc(base_summed, 1)
                    if u == 3 and not isinstance(it, int):
                        add_down_group(2 * it - 1)
                    if u == SLOTS + 3:
                        if isinstance(it, int):
                            dve.wait_ge(base_ready, 2)
                        add_down_group(2 * it)

            turn(0)
            with dve.Fori(1, TURNS) as it:
                turn(it)

            def finish_unit(v):
                half, b, i0 = v // UP_UNITS, v % UP_UNITS // (I // UP_I), v % (I // UP_I) * UP_I
                place = xs[:, b, i0:i0 + UP_I, half * HALF:(half + 1) * HALF]
                dve.wait_ge(bu_added, I * (b + 1))
                dve.wait_ge(up_summed, v + 1)
                nc.vector.tensor_tensor(place, bank[v % BANK_RING][:].rearrange("p (i d) -> p i d", d=HALF),
                                        place, ALU.add).then_inc(unit_final, 1)

            for t in range(CHUNKS):
                c = CHUNKS + t
                transpose_b(c, t % W_RING, 16 * (c // W_RING + 1))
                if 1 <= t <= FULL_FROM:
                    n = (t - 1) % 2
                    dve.wait_ge(hiA_ready, t)
                    nc.vector.tensor_tensor(loA[:, n], tA[:, n], hiA[:, n].bitcast(fp32),
                                            ALU.subtract).then_inc(loA_ready, 1)
                transpose_a(c, t % W_RING)
                if t % SLOTS == 3:
                    g = c // SLOTS - 1
                    add_down_group(g) if g < GROUPS else add_up_group(g)
                for at in (UP_AT_A, UP_AT_B):
                    if t - UP_LAG in at:
                        finish_unit(at[t - UP_LAG])
            for t in range(CHUNKS, CHUNKS + UP_LAG):
                for at in (UP_AT_A, UP_AT_B):
                    if t - UP_LAG in at:
                        finish_unit(at[t - UP_LAG])
            add_up_group(2 * GROUPS - 1)
            for v in range(UP_UNITS, 2 * UP_UNITS):
                finish_unit(v)

        @block.scalar
        def _(act):
            act.wait_ge(stationaries_zeroed, 2)
            act.wait_ge(h_copied, 3)
            for q in range(Q):
                nc.scalar.activation(place(st_split, 0, q), spread(h_hi, q, R), ACT.Copy
                                     ).then_inc(split_ready, 1)
                nc.scalar.activation(place(st_split, 1, q), spread(h_lo, q, R), ACT.Copy
                                     ).then_inc(split_ready, 1)

            def round_b(c, slot):
                act.wait_ge(tB_ready, c + 1)
                if later(c, 2):
                    act.wait_ge(sumB_done, c - 1)
                nc.scalar.activation(hiB[:, slot % 2], tB[:, slot % 2], ACT.Copy).then_inc(hiB_ready, 1)

            def copy_group(g, n):
                act.wait_ge(sumB_done, SLOTS * (g + 1))
                if later(g, 2):
                    act.wait_ge(g_turned, g - 1)
                nc.scalar.activation(g_rows[:, n].rearrange("p (j k) -> p j k", k=K),
                                     acc[n][:].rearrange("p (k j) -> p j k", k=K),
                                     ACT.Copy, scale=DELTA_SCALE).then_inc(g_ready, 1)

            def turn(it):
                for u in range(GROUP_CHUNKS_LOOPED):
                    round_b(GROUP_CHUNKS_LOOPED * it + u, u)
                    if u == 1 and not isinstance(it, int):
                        copy_group(2 * it - 1, 1)
                    if u == 5 and isinstance(it, int):
                        act.wait_ge(base_turned, 1)
                        nc.scalar.activation(base_d[:], bank[0][:].rearrange("p (c n) -> p c n", c=C),
                                             ACT.Copy).then_inc(base_ready, 1)
                        act.wait_ge(base_turned, 2)
                        nc.scalar.activation(base_u[:], bank[1][:], ACT.Copy).then_inc(base_ready, 1)
                    if u == SLOTS + 1:
                        copy_group(2 * it, 0)

            turn(0)
            with act.Fori(1, TURNS) as it:
                turn(it)

            def copy_x(m):
                j, c0 = m // 2, m % 2 * BANK_C
                act.wait_ge(x_turned, m + 1)
                if j >= XT_RING:
                    act.wait_ge(down_summed, j - XT_RING + 1)
                nc.scalar.activation(xt[:, j % XT_RING, c0:c0 + BANK_C, :],
                                     bank[m % BANK_RING][:].rearrange("p (c l) -> p c l", c=BANK_C),
                                     ACT.Copy).then_inc(x_copied, 1)

            def copy_down(j):
                act.wait_ge(down_summed, j + 1)
                b, i0 = j // BATCH_UNITS, j % BATCH_UNITS * UNIT_I
                nc.scalar.activation(down[:, b, i0:i0 + UNIT_I, :],
                                     dn[:].rearrange("p (i l) -> p i l", i=UNIT_I),
                                     ACT.Relu, bias=bd_col[:]).then_inc(down_ready, 1)

            for t in range(CHUNKS):
                c = CHUNKS + t
                round_b(c, t)
                if t < FULL_FROM:
                    act.wait_ge(tA_ready, c + 1)
                    act.wait_ge(sumA_done, c - 1)
                    nc.scalar.activation(hiA[:, t % 2], tA[:, t % 2], ACT.Copy).then_inc(hiA_ready, 1)
                if 0 <= t - X_LAG < X_BANKS // 2:
                    copy_x(2 * (t - X_LAG))
                    copy_x(2 * (t - X_LAG) + 1)
                if t - 1 in DOWN_AT:
                    copy_down(DOWN_AT[t - 1])
                if t == FULL_FROM - 1:
                    act.wait_ge(stationaries_zeroed, 3)
                    for q in range(Q):
                        nc.scalar.activation(place(st_full2, 0, q), spread(h32, q, 2), ACT.Copy
                                             ).then_inc(full_ready, 1)
                if t % SLOTS == 1:
                    g = c // SLOTS - 1
                    copy_group(g, g % 2)
            copy_group(2 * GROUPS - 1, 1)

        @block.gpsimd
        def _(pool):
            nc.gpsimd.memset(ident[:], 0.0).then_inc(ident_zeroed, 1)
            pool.wait_ge(ident_zeroed, 1)
            nc.gpsimd.affine_select(out=ident[:], in_=ident[:], compare_op=ALU.not_equal, fill=1.0,
                                    base=0, pattern=[[-1, P]], channel_multiplier=1
                                    ).then_inc(ident_ready, 1)
            nc.gpsimd.memset(st_full[:], 0.0).then_inc(stationaries_zeroed, 1)
            nc.gpsimd.memset(st_split[:].bitcast(fp32), 0.0).then_inc(stationaries_zeroed, 1)

            def rest_b(c, slot):
                pool.wait_ge(hiB_ready, c + 1)
                nc.gpsimd.tensor_tensor(loB[:, slot % 2], tB[:, slot % 2], hiB[:, slot % 2].bitcast(fp32),
                                        ALU.subtract).then_inc(loB_ready, 1)

            def turn(it):
                for u in range(GROUP_CHUNKS_LOOPED):
                    rest_b(GROUP_CHUNKS_LOOPED * it + u, u)

            turn(0)
            with pool.Fori(1, TURNS) as it:
                turn(it)
            for t in range(CHUNKS):
                rest_b(CHUNKS + t, t)
                if t == FULL_FROM - 1:
                    pool.wait_ge(down_summed, DOWN_UNITS)
                    nc.gpsimd.memset(st_full2, 0.0).then_inc(stationaries_zeroed, 1)
                for piece in range(BU_PIECES):
                    if BU_AT[piece] == t:
                        b, i = piece // I, piece % I
                        pool.wait_ge(x_turned, 2 * (piece // UNIT_I + 1))
                        nc.gpsimd.tensor_tensor(xs[:, b, i], xs[:, b, i], bu_all[:], ALU.add
                                                ).then_inc(bu_added, 1)

        @block.tensor
        def _(pe):
            pe.wait_ge(cond_spread, 1)
            pe.wait_ge(ident_ready, 1)
            for r in range(R):
                last = nc.tensor.transpose(gt[:, 0, r * B:(r + 1) * B],
                                           cond_rep[:, r].rearrange("b q i -> b (q i)"), ident[0:B, 0:B])
            last.then_inc(cond_turned, 1)

            def stationary(st, r, s):
                return st[:, r, s * P:(s + 1) * P]

            def sum_a_full(c, u, a, st):
                s = u % SLOTS
                pe.wait_ge(tA_ready, c + 1)
                nc.tensor.matmul(a, stationary(st, 0, s), tA[:, u % 2, 0], start=s == 0, stop=False)
                nc.tensor.matmul(a, stationary(st, 1, s), tA[:, u % 2, 1], start=False, stop=False
                                 ).then_inc(sumA_done, 1)

            def add_split(a, moving, r, s, start=False, stop=False):
                return nc.tensor.matmul(a, stationary(st_split, r, s), moving, start=start, stop=stop)

            def sum_b(c, u, a):
                s = u % SLOTS
                pe.wait_ge(hiB_ready, c + 1)
                add_split(a, hiB[:, u % 2, 0], 2, s)
                add_split(a, hiB[:, u % 2, 1], 3, s)
                pe.wait_ge(loB_ready, c + 1)
                add_split(a, loB[:, u % 2, 0], 2, s)
                add_split(a, loB[:, u % 2, 1], 3, s, stop=s == SLOTS - 1).then_inc(sumB_done, 1)

            def turn_group(g, n):
                pe.wait_ge(g_ready, g + 1)
                if later(g, 1):
                    pe.wait_ge(group_added, g)
                for k in range(C):
                    last = nc.tensor.transpose(gt[:, k], g_rows[:, n, k * P:(k + 1) * P], ident[:])
                last.then_inc(g_turned, 1)

            pe.wait_ge(full_ready, Q)

            def turn(it):
                for u in range(GROUP_CHUNKS_LOOPED):
                    c, s, n = GROUP_CHUNKS_LOOPED * it + u, u % SLOTS, u // SLOTS
                    if s == 0 and later(it, 1):
                        pe.wait_ge(g_ready, 2 * it + n - 1)
                    sum_a_full(c, u, acc[n][:], st_full)
                    if u == 0 and isinstance(it, int):
                        pe.wait_ge(split_ready, 2 * Q)
                    sum_b(c, u, acc[n][:])
                    if u == 4 and isinstance(it, int):
                        for k, (b, nat_w) in enumerate(((bank[0], wd_nat), (bank[1], wu_nat))):
                            pe.wait_ge(base_summed, k + 1)
                            for cc in range(C):
                                last = nc.tensor.transpose(b[:, cc * P:(cc + 1) * P], nat_w[:, cc], ident[:])
                            last.then_inc(base_turned, 1)
                    if u == 1 and not isinstance(it, int):
                        turn_group(2 * it - 1, 1)
                    if u == SLOTS + 1:
                        turn_group(2 * it, 0)

            turn(0)
            with pe.Fori(1, TURNS) as it:
                turn(it)

            def turn_x(m):
                j, c0 = m // 2, m % 2 * BANK_C
                b, i0 = j // BATCH_UNITS, j % BATCH_UNITS * UNIT_I
                pe.wait_ge(x_loaded[(b * I + i0) * X_PIECES // (B * I)], 16)
                if m >= BANK_RING:
                    pe.wait_ge(x_copied, m - BANK_RING + 1)
                for n, (c, i) in enumerate((c, i) for c in range(c0, c0 + BANK_C) for i in range(UNIT_I)):
                    last = nc.tensor.transpose(bank[m % BANK_RING][:, n * P:(n + 1) * P],
                                               xs[:, b, i0 + i, c * P:(c + 1) * P], ident[:])
                last.then_inc(x_turned, 1)

            def down_unit(j):
                pe.wait_ge(group_added, GROUPS)
                pe.wait_ge(x_copied, 2 * (j + 1))
                if j >= 1:
                    pe.wait_ge(down_ready, j)
                for c in range(C):
                    last = nc.tensor.matmul(dn[:], wd_b[:, c, j // BATCH_UNITS], xt[:, j % XT_RING, c],
                                            start=c == 0, stop=c == C - 1)
                last.then_inc(down_summed, 1)

            def up_unit(v):
                half, b, i0 = v // UP_UNITS, v % UP_UNITS // (I // UP_I), v % (I // UP_I) * UP_I
                pe.wait_ge(group_added, GROUPS + (half + 1) * GROUPS // 2)
                pe.wait_ge(down_ready, (b * I + i0 + UP_I) // UNIT_I)
                if v == 0:
                    pe.wait_ge(x_copied, X_BANKS)
                if v >= BANK_RING:
                    pe.wait_ge(unit_final, v - BANK_RING + 1)
                for i in range(UP_I):
                    last = nc.tensor.matmul(bank[v % BANK_RING][:, i * HALF:(i + 1) * HALF],
                                            down[:, b, i0 + i], wu_b[:, b, half * HALF:(half + 1) * HALF],
                                            start=True, stop=True)
                last.then_inc(up_summed, 1)

            for t in range(CHUNKS):
                c, s, n = CHUNKS + t, t % SLOTS, t // SLOTS % 2
                if s == 0:
                    pe.wait_ge(g_ready, c // SLOTS - 1)
                pe.wait_ge(tA_ready, c + 1)
                if t < FULL_FROM:
                    pe.wait_ge(hiA_ready, t + 1)
                    add_split(acc[n][:], hiA[:, t % 2, 0], 0, s, start=s == 0)
                    add_split(acc[n][:], hiA[:, t % 2, 1], 1, s)
                    pe.wait_ge(loA_ready, t + 1)
                    add_split(acc[n][:], loA[:, t % 2, 0], 0, s)
                    add_split(acc[n][:], loA[:, t % 2, 1], 1, s).then_inc(sumA_done, 1)
                else:
                    pe.wait_ge(full_ready, 2 * Q)
                    sum_a_full(c, t, acc[n][:], st_full2)
                if t < X_BANKS // 2:
                    turn_x(2 * t)
                if t in DOWN_AT:
                    down_unit(DOWN_AT[t])
                if t in UP_AT_A:
                    up_unit(UP_AT_A[t])
                if s == 1:
                    g = c // SLOTS - 1
                    turn_group(g, g % 2)
                sum_b(c, t, acc[n][:])
                if t < X_BANKS // 2:
                    turn_x(2 * t + 1)
                if t in UP_AT_B:
                    up_unit(UP_AT_B[t])
            turn_group(2 * GROUPS - 1, 1)
            for v in range(UP_UNITS, 2 * UP_UNITS):
                up_unit(v)


_INS = ['x', 'cond_256', 'L0_cond_Wd', 'L0_cond_bd', 'L0_cond_Wu', 'L0_cond_bu',
        'L0_cond_Wdd', 'L0_cond_bdd', 'L0_cond_Wdu', 'L0_cond_bdu']
_OUTS = [((B, L, D), 'float32')]


def kernel(**inputs):
    import numpy as _np
    import concourse.bacc as _bacc
    from concourse import mybir as _mybir
    from concourse.bass_utils import run_bass_kernel_spmd as _run

    nc = _bacc.Bacc("TRN2", target_bir_lowering=False, num_devices=1)
    arrays, args = {}, []
    for name in _INS:
        a = _np.ascontiguousarray(inputs[name])
        arrays[f"in_{name}_dram"] = a
        args.append(nc.dram_tensor(f"in_{name}_dram", a.shape, _mybir.dt.from_np(a.dtype), kind="ExternalInput").ap())
    for i, (shape, dtype) in enumerate(_OUTS):
        dt = _mybir.dt.from_np(_np.dtype(dtype))
        args.append(nc.dram_tensor(f"out_{i}_dram", shape, dt, kind="ExternalOutput").ap())
    hyper_adapter(nc, *args)
    r = _run(nc, [arrays], core_ids=[0])
    return r.results[0]["out_0_dram"]
```

```python
from contextlib import ExitStack

import concourse.bass as bass
from concourse import mybir

P = 128
QUAD = 32
B, L, D, N, H = 4, 1024, 512, 128, 128
DELTA_SCALE = 0.1

K = 16
CHUNK_ROWS = P * K
R = H // QUAD
Q = P // QUAD
COLS = K * QUAD
SLOTS = 4
CHUNKS = D * N // CHUNK_ROWS
GROUPS = CHUNKS // SLOTS
GROUP_CHUNKS_LOOPED = 2 * SLOTS
TURNS = CHUNKS // GROUP_CHUNKS_LOOPED
SQ = SLOTS * Q
PART = SQ * B
FILL = SLOTS * P + SQ * B
FILL_STEP = P + Q * B
W_RING = 4

C = D // P
I = L // P
UNIT_I = 2
DOWN_UNITS = B * I // UNIT_I
BATCH_UNITS = I // UNIT_I
BANK_C = 2
BANK_RING = 4
X_BANKS = DOWN_UNITS * C // BANK_C
HALF = D // 2
UP_I = 2
UP_UNITS = B * I // UP_I

X_LAG = 2
XT_RING = 3
DOWN_AT = {j + 3: j for j in range(DOWN_UNITS)}
UP_START = 19
UP_AT_A = {}
UP_AT_B = {}
_v = 0
for _t in range(UP_START, CHUNKS):
    if _t % 4 == 2 and _v < UP_UNITS:
        UP_AT_A[_t] = _v
        _v += 1
    if _v < UP_UNITS:
        UP_AT_B[_t] = _v
        _v += 1
assert _v == UP_UNITS
UP_LAG = 2
BU_AT = 3
BU_DVE_UNITS = UP_UNITS // 2
BU_DVE_AT = CHUNKS - BU_DVE_UNITS // 2
X_PIECES = 2 * B
X_LOAD_AT = {0: 0, **{2 * h + 1: h for h in range(1, X_PIECES)}}
BOTH_FROM = 2
ONE_FROM = 22


def later(count, back):
    return not isinstance(count, int) or count >= back


def hyper_adapter(nc, x, cond, Wd, bd, Wu, bu, Wdd, bdd, Wdu, bdu, out):
    fp32, fp32r = mybir.dt.float32, mybir.dt.float32r
    ALU = mybir.AluOpType
    ACT = mybir.ActivationFunctionType

    wdd_chunks = Wdd.rearrange("(c p k) h -> c p (k h)", p=P, k=K)
    wdu_chunks = Wdu.rearrange("(c p k) h -> c p (k h)", p=P, k=K)
    x_rows = x.rearrange("b (p i) d -> b p i d", p=P)
    out_rows = out.rearrange("b (p i) d -> b p i d", p=P)

    ctx = ExitStack()
    with ctx:
        def sb(name, shape, dt=fp32):
            return ctx.enter_context(nc.sbuf_tensor(name, shape, dt))

        def pb(name, shape, dt=fp32):
            return ctx.enter_context(nc.psum_tensor(name, shape, dt))

        def sem(name):
            return ctx.enter_context(nc.semaphore(name))

        xs = sb("xs", [P, B, I, D])
        w = sb("w", [P, W_RING, K * H])
        tA = sb("tA", [P, 2, 2, COLS])
        tB = sb("tB", [P, 2, 2, COLS])
        hiA = sb("hiA", [P, 2, 2, COLS], fp32r)
        loA = sb("loA", [P, 2, 2, COLS], fp32r)
        hiB = sb("hiB", [P, 2, 2, COLS], fp32r)
        loB = sb("loB", [P, 2, 2, COLS], fp32r)
        g_rows = sb("g_rows", [P, 2, COLS])
        wd_b = sb("wd_b", [P, C, B, N])
        wu_b = sb("wu_b", [P, B, D])
        down = sb("down", [P, B, I, P])
        xt = sb("xt", [P, XT_RING, C, UNIT_I * P])
        base_u = sb("base_u", [P, D])
        st_split = sb("st_split", [P, R, FILL], fp32r)
        ident = sb("ident", [P, P])
        bu_all = sb("bu_all", [P, D])
        bd_col = sb("bd_col", [P, 1])
        h32 = sb("h32", [P, R, B])
        h_hi = sb("h_hi", [P, R, B], fp32r)
        h_lo = sb("h_lo", [P, R, B], fp32r)
        cond_rows = xt[0:B, 0, 0, 0:H].rearrange("b (r i) -> b r i", i=QUAD)
        cond_rep = xt[0:B, 0, 1:3, :].rearrange("b c (r q i) -> b (c r) q i", q=Q, i=QUAD)
        st_full = xs[:, B - 1, 0:3, :].rearrange("p i d -> p (i d)")[:, 0:2 * FILL].rearrange(
            "p (r z) -> p r z", z=FILL)
        base_d = xs[:, B - 1, 3, :].rearrange("p (c n) -> p c n", c=C)
        st_full2 = wd_b[:].rearrange("p c b n -> p (c b n)")[:, 0:FILL].rearrange(
            "p (r z) -> p r z", z=FILL)
        nat = [down[:, b, 0:C, :] for b in range(B)]
        wd_nat, bdd_nat, wu_nat, bdu_nat = nat

        acc = [pb(f"acc{n}", [P, COLS]) for n in range(2)]
        gt = pb("gt", [P, C, P])
        dn = pb("dn", [P, UNIT_I * P])
        bank = [pb(f"bank{n}", [P, UP_I * HALF]) for n in range(BANK_RING)]

        cond_loaded = sem("cond_loaded")
        base_d_loaded = sem("base_d_loaded")
        base_u_loaded = sem("base_u_loaded")
        w_loaded = [sem(f"w_loaded{n}") for n in range(W_RING)]
        x_loaded = [sem(f"x_loaded{h}") for h in range(X_PIECES)]
        ident_zeroed = sem("ident_zeroed")
        ident_ready = sem("ident_ready")
        stationaries_zeroed = sem("stationaries_zeroed")
        cond_spread = sem("cond_spread")
        cond_turned = sem("cond_turned")
        h_copied = sem("h_copied")
        full_ready = sem("full_ready")
        split_ready = sem("split_ready")
        base_summed = sem("base_summed")
        base_turned = sem("base_turned")
        base_ready = sem("base_ready")
        tA_ready = sem("tA_ready")
        tB_ready = sem("tB_ready")
        hiA_ready = sem("hiA_ready")
        hiB_ready = sem("hiB_ready")
        loA_ready = sem("loA_ready")
        loB_ready = sem("loB_ready")
        sumA_done = sem("sumA_done")
        sumB_done = sem("sumB_done")
        g_ready = sem("g_ready")
        g_turned = sem("g_turned")
        part1_added = sem("part1_added")
        group_added = sem("group_added")
        x_turned = sem("x_turned")
        x_copied = sem("x_copied")
        down_summed = sem("down_summed")
        down_ready = sem("down_ready")
        bu_added = sem("bu_added")
        bu_added_late = sem("bu_added_late")
        up_summed = sem("up_summed")
        unit_final = sem("unit_final")
        out_stored = sem("out_stored")

        block = ctx.enter_context(nc.Block())

        def place(st, part, q):
            v = st[QUAD * q:QUAD * (q + 1)].rearrange("p r (s z) -> p r s z", z=FILL_STEP)
            return v[:, :, :, part * PART + q * B:part * PART + (q + 1) * B]

        def unit_x(v):
            half, b, i0 = v // UP_UNITS, v % UP_UNITS // (I // UP_I), v % (I // UP_I) * UP_I
            return xs[:, b, i0:i0 + UP_I, half * HALF:(half + 1) * HALF]

        def unit_bu(v):
            half = v // UP_UNITS
            bu_half = bu_all[:, half * HALF:(half + 1) * HALF]
            return bu_half.unsqueeze(1).to_broadcast([P, UP_I, HALF])

        def spread(h, q, quarters):
            rows = h[QUAD * q:QUAD * (q + 1), 0:quarters]
            return rows.unsqueeze(2).to_broadcast([QUAD, quarters, SLOTS, B])

        @block.sync
        def _(sp):
            def load_chunk(c, chunk, slot):
                if later(c, W_RING):
                    sp.wait_ge(tA_ready, c - W_RING + 1)
                sp.dma_start(w[:, slot, :], chunk).then_inc(w_loaded[slot], 16)

            def load_x(h):
                i = slice(h % 2 * I // 2, (h % 2 + 1) * I // 2)
                sp.dma_start(xs[:, h // 2, i], x_rows[h // 2, :, i]).then_inc(x_loaded[h], 16)

            def turn(it):
                for u in range(GROUP_CHUNKS_LOOPED):
                    c = GROUP_CHUNKS_LOOPED * it + u
                    load_chunk(c, wdd_chunks[c], u % W_RING)
                    if u == 1 and isinstance(it, int):
                        load_base_d()

            def load_base_d():
                sp.dma_start(wd_nat, Wd.rearrange("n (c d) -> n c d", c=C)).then_inc(base_d_loaded, 16)
                sp.dma_start(bdd_nat, bdd.rearrange("(n c d) -> n c d", c=C, d=P)).then_inc(base_d_loaded, 16)

            def load_base_u():
                sp.dma_start(wu_nat, Wu.rearrange("(c d) n -> d c n", c=C)).then_inc(base_u_loaded, 16)
                sp.dma_start(bdu_nat, bdu.rearrange("(c d n) -> d c n", c=C, n=N)).then_inc(base_u_loaded, 16)
                sp.dma_start(bu_all[:], bu.rearrange("(o d) -> o d", o=1).to_broadcast([P, D])
                             ).then_inc(base_u_loaded, 16)
                sp.dma_start(bd_col[:], bd.rearrange("(p o) -> p o", o=1)).then_inc(base_u_loaded, 16)

            sp.dma_start(cond_rows, cond.rearrange("b (r i) -> b r i", i=QUAD)).then_inc(cond_loaded, 16)
            turn(0)
            with sp.Fori(1, TURNS) as it:
                turn(it)

            def store(v, units):
                half, b, i0 = v // UP_UNITS, v % UP_UNITS // (I // UP_I), v % (I // UP_I) * UP_I
                i0 -= (units - 1) * UP_I
                sp.wait_ge(unit_final, v + 1)
                sp.dma_start(out_rows[b, :, i0:i0 + units * UP_I, half * HALF:(half + 1) * HALF],
                             xs[:, b, i0:i0 + units * UP_I, half * HALF:(half + 1) * HALF]
                             ).then_inc(out_stored, 16)

            stores = 0
            at = {t: v for d in (UP_AT_A, UP_AT_B) for t, v in d.items() if v % 4 == 3}
            for t in range(CHUNKS):
                if t in X_LOAD_AT:
                    load_x(X_LOAD_AT[t])
                if t == 1:
                    load_base_u()
                load_chunk(CHUNKS + t, wdu_chunks[t], t % W_RING)
                if t - UP_LAG - W_RING - 1 in at:
                    store(at.pop(t - UP_LAG - W_RING - 1), 4)
                    stores += 1
            for t in sorted(at):
                store(at[t], 4)
                stores += 1
            for v in range(UP_UNITS + 1, 2 * UP_UNITS - 2, 2):
                store(v, 2)
                stores += 1
            for v in range(2 * UP_UNITS - 2, 2 * UP_UNITS):
                store(v, 1)
                stores += 1
            sp.wait_ge(out_stored, 16 * stores)

        @block.vector
        def _(dve):
            dve.wait_ge(cond_loaded, 16)
            nc.vector.tensor_copy(cond_rep, cond_rows.unsqueeze(2).to_broadcast([B, R, Q, QUAD])
                                  ).then_inc(cond_spread, 1)
            dve.wait_ge(cond_turned, 1)
            nc.vector.tensor_copy(h32[:], gt[:, 0, 0:R * B].rearrange("p (r b) -> p r b", b=B)
                                  ).then_inc(h_copied, 1)
            dve.wait_ge(h_copied, 1)
            nc.vector.tensor_copy(h_hi[:], h32[:]).then_inc(h_copied, 1)
            dve.wait_ge(h_copied, 2)
            nc.vector.tensor_tensor(h_lo[:], h32[:], h_hi[:].bitcast(fp32), ALU.subtract
                                    ).then_inc(h_copied, 1)
            dve.wait_ge(h_copied, 3)
            dve.wait_ge(stationaries_zeroed, 1)
            for q in range(Q):
                nc.vector.tensor_copy(place(st_full, 0, q), spread(h32, q, 2)).then_inc(full_ready, 1)

            def quarters(slot, r):
                chunk = w[:, slot, :].rearrange("p (k r h) -> p k r h", r=R, h=QUAD)
                return chunk[:, :, r:r + 2, :]

            def transpose_b(c, slot, loaded):
                dve.wait_ge(w_loaded[slot], loaded)
                if later(c, 2):
                    dve.wait_ge(loB_ready, c - 1)
                nc.vector.transpose(tB[:, slot % 2].rearrange("p r (k j) -> p k r j", j=QUAD),
                                    quarters(slot, 2)).then_inc(tB_ready, 1)

            def transpose_a(c, slot):
                if later(c, 2):
                    dve.wait_ge(sumA_done, c - 1)
                nc.vector.transpose(tA[:, slot % 2].rearrange("p r (k j) -> p k r j", j=QUAD),
                                    quarters(slot, 0)).then_inc(tA_ready, 1)

            def add_group(g, parts, base, total):
                dve.wait_ge(g_turned, g + 1)
                nc.vector.tensor_tensor(total, parts[1], base, ALU.add).then_inc(part1_added, 1)
                dve.wait_ge(part1_added, g + 1)
                nc.vector.tensor_tensor(total, parts[0], total, ALU.add).then_inc(group_added, 1)

            def turned_parts():
                v = gt[:].rearrange("p c (a s b) -> p c a s b", s=SQ, b=B)
                return [v[:, :, a] for a in range(2)]

            def add_down_group(g):
                n = bass.ds(g * SQ, SQ)
                total = wd_b[:, :, :, n].rearrange("p c b s -> p c s b")
                base = base_d[:, :, n].unsqueeze(3).to_broadcast([P, C, SQ, B])
                add_group(g, turned_parts(), base, total)

            def add_up_group(g):
                d = slice((g - GROUPS) * D // GROUPS, (g - GROUPS + 1) * D // GROUPS)
                total = wu_b[:, :, d].rearrange("p b (s c) -> p c s b", c=C)
                base = base_u[:, d].rearrange("p (s c) -> p c s", c=C)
                add_group(g, turned_parts(), base.unsqueeze(3).to_broadcast([P, C, SQ, B]), total)

            def turn(it):
                for u in range(GROUP_CHUNKS_LOOPED):
                    c = GROUP_CHUNKS_LOOPED * it + u
                    transpose_b(c, u % W_RING, 16 * (2 * it + u // W_RING + 1))
                    transpose_a(c, u % W_RING)
                    if u == 3 and isinstance(it, int):
                        dve.wait_ge(base_d_loaded, 16 * 2)
                        nc.vector.scalar_tensor_tensor(wd_nat, bdd_nat, DELTA_SCALE, wd_nat,
                                                       ALU.mult, ALU.add).then_inc(base_summed, 1)
                    if u == 3 and not isinstance(it, int):
                        add_down_group(2 * it - 1)
                    if u == SLOTS + 3:
                        if isinstance(it, int):
                            dve.wait_ge(base_ready, 1)
                        add_down_group(2 * it)

            turn(0)
            with dve.Fori(1, TURNS) as it:
                turn(it)

            def add_bu_late(n):
                dve.wait_ge(x_turned, X_BANKS)
                nc.vector.tensor_tensor(unit_x(UP_UNITS + n), unit_x(UP_UNITS + n),
                                        unit_bu(UP_UNITS + n), ALU.add).then_inc(bu_added_late, 1)

            def finish_unit(v):
                place = unit_x(v)
                if UP_UNITS <= v < UP_UNITS + BU_DVE_UNITS:
                    dve.wait_ge(bu_added_late, v - UP_UNITS + 1)
                else:
                    dve.wait_ge(bu_added, v + 1 if v < UP_UNITS else v + 1 - BU_DVE_UNITS)
                dve.wait_ge(up_summed, v + 1)
                nc.vector.tensor_tensor(place, bank[v % BANK_RING][:].rearrange("p (i d) -> p i d", d=HALF),
                                        place, ALU.add).then_inc(unit_final, 1)

            for t in range(CHUNKS):
                c = CHUNKS + t
                transpose_b(c, t % W_RING, 16 * (c // W_RING + 1))
                if BOTH_FROM < t <= ONE_FROM:
                    n = (t - 1) % 2
                    dve.wait_ge(hiA_ready, t - BOTH_FROM)
                    nc.vector.tensor_tensor(loA[:, n], tA[:, n], hiA[:, n].bitcast(fp32),
                                            ALU.subtract).then_inc(loA_ready, 1)
                transpose_a(c, t % W_RING)
                if t == 2:
                    dve.wait_ge(base_u_loaded, 16 * 4)
                    nc.vector.scalar_tensor_tensor(wu_nat, bdu_nat, DELTA_SCALE, wu_nat,
                                                   ALU.mult, ALU.add).then_inc(base_summed, 1)
                if t >= BU_DVE_AT:
                    add_bu_late(t - BU_DVE_AT)
                if t == 2 * SLOTS - 1:
                    dve.wait_ge(base_ready, 2)
                if t % SLOTS == 3:
                    g = c // SLOTS - 1
                    add_down_group(g) if g < GROUPS else add_up_group(g)
                for at in (UP_AT_A, UP_AT_B):
                    if t - UP_LAG in at:
                        finish_unit(at[t - UP_LAG])
            for n in range(CHUNKS - BU_DVE_AT, BU_DVE_UNITS):
                add_bu_late(n)
            for t in range(CHUNKS, CHUNKS + UP_LAG):
                if t == CHUNKS + UP_LAG - 1:
                    add_up_group(2 * GROUPS - 1)
                for at in (UP_AT_A, UP_AT_B):
                    if t - UP_LAG in at:
                        finish_unit(at[t - UP_LAG])
            for v in range(UP_UNITS, 2 * UP_UNITS):
                finish_unit(v)

        @block.scalar
        def _(act):
            act.wait_ge(stationaries_zeroed, 2)
            act.wait_ge(h_copied, 3)
            for q in range(Q):
                nc.scalar.activation(place(st_split, 0, q), spread(h_hi, q, R), ACT.Copy
                                     ).then_inc(split_ready, 1)
                nc.scalar.activation(place(st_split, 1, q), spread(h_lo, q, R), ACT.Copy
                                     ).then_inc(split_ready, 1)

            def round_b(c, slot):
                act.wait_ge(tB_ready, c + 1)
                if later(c, 2):
                    act.wait_ge(sumB_done, c - 1)
                nc.scalar.activation(hiB[:, slot % 2], tB[:, slot % 2], ACT.Copy).then_inc(hiB_ready, 1)

            def copy_group(g, n):
                act.wait_ge(sumA_done, SLOTS * (g + 1))
                act.wait_ge(sumB_done, SLOTS * (g + 1))
                if later(g, 2):
                    act.wait_ge(g_turned, g - 1)
                nc.scalar.activation(g_rows[:, n].rearrange("p (j k) -> p j k", k=K),
                                     acc[n][:].rearrange("p (k j) -> p j k", k=K),
                                     ACT.Copy, scale=DELTA_SCALE).then_inc(g_ready, 1)

            def turn(it):
                for u in range(GROUP_CHUNKS_LOOPED):
                    round_b(GROUP_CHUNKS_LOOPED * it + u, u)
                    if u == 1 and not isinstance(it, int):
                        copy_group(2 * it - 1, 1)
                    if u == 5 and isinstance(it, int):
                        act.wait_ge(base_turned, 1)
                        nc.scalar.activation(base_d[:], bank[0][:].rearrange("p (c n) -> p c n", c=C),
                                             ACT.Copy).then_inc(base_ready, 1)
                    if u == SLOTS + 1:
                        copy_group(2 * it, 0)

            turn(0)
            with act.Fori(1, TURNS) as it:
                turn(it)

            def copy_x(m):
                j, c0 = m // 2, m % 2 * BANK_C
                act.wait_ge(x_turned, m + 1)
                if j >= XT_RING:
                    act.wait_ge(down_summed, j - XT_RING + 1)
                nc.scalar.activation(xt[:, j % XT_RING, c0:c0 + BANK_C, :],
                                     bank[m % BANK_RING][:].rearrange("p (c l) -> p c l", c=BANK_C),
                                     ACT.Copy).then_inc(x_copied, 1)

            def copy_down(j):
                act.wait_ge(down_summed, j + 1)
                b, i0 = j // BATCH_UNITS, j % BATCH_UNITS * UNIT_I
                nc.scalar.activation(down[:, b, i0:i0 + UNIT_I, :],
                                     dn[:].rearrange("p (i l) -> p i l", i=UNIT_I),
                                     ACT.Relu, bias=bd_col[:]).then_inc(down_ready, 1)

            for t in range(CHUNKS):
                c = CHUNKS + t
                round_b(c, t)
                if t >= BOTH_FROM:
                    r = 0 if t < ONE_FROM else 1
                    act.wait_ge(tA_ready, c + 1)
                    act.wait_ge(sumA_done, c - 1)
                    nc.scalar.activation(hiA[:, t % 2, r:2], tA[:, t % 2, r:2], ACT.Copy
                                         ).then_inc(hiA_ready, 1)
                if t == SLOTS + 1:
                    act.wait_ge(base_turned, 2)
                    nc.scalar.activation(base_u[:], gt[:].rearrange("p c n -> p (c n)"), ACT.Copy
                                         ).then_inc(base_ready, 1)
                if 0 <= t - X_LAG < X_BANKS // 2:
                    copy_x(2 * (t - X_LAG))
                    copy_x(2 * (t - X_LAG) + 1)
                if t - 1 in DOWN_AT:
                    copy_down(DOWN_AT[t - 1])
                if t == ONE_FROM - 1:
                    act.wait_ge(stationaries_zeroed, 3)
                    for q in range(Q):
                        nc.scalar.activation(place(st_full2, 0, q), spread(h32, q, 1), ACT.Copy
                                             ).then_inc(full_ready, 1)
                if t % SLOTS == 1:
                    g = c // SLOTS - 1
                    copy_group(g, g % 2)
            copy_group(2 * GROUPS - 1, 1)

        @block.gpsimd
        def _(pool):
            nc.gpsimd.memset(ident[:], 0.0).then_inc(ident_zeroed, 1)
            pool.wait_ge(ident_zeroed, 1)
            nc.gpsimd.affine_select(out=ident[:], in_=ident[:], compare_op=ALU.not_equal, fill=1.0,
                                    base=0, pattern=[[-1, P]], channel_multiplier=1
                                    ).then_inc(ident_ready, 1)
            nc.gpsimd.memset(st_full[:], 0.0).then_inc(stationaries_zeroed, 1)
            nc.gpsimd.memset(st_split[:].bitcast(fp32), 0.0).then_inc(stationaries_zeroed, 1)

            def rest_b(c, slot):
                pool.wait_ge(hiB_ready, c + 1)
                nc.gpsimd.tensor_tensor(loB[:, slot % 2], tB[:, slot % 2], hiB[:, slot % 2].bitcast(fp32),
                                        ALU.subtract).then_inc(loB_ready, 1)

            def turn(it):
                for u in range(GROUP_CHUNKS_LOOPED):
                    rest_b(GROUP_CHUNKS_LOOPED * it + u, u)

            turn(0)
            with pool.Fori(1, TURNS) as it:
                turn(it)

            def add_bu(v):
                nc.gpsimd.tensor_tensor(unit_x(v), unit_x(v), unit_bu(v), ALU.add).then_inc(bu_added, 1)

            for t in range(CHUNKS):
                rest_b(CHUNKS + t, t)
                if t >= ONE_FROM:
                    pool.wait_ge(hiA_ready, t - BOTH_FROM + 1)
                    nc.gpsimd.tensor_tensor(loA[:, t % 2, 1], tA[:, t % 2, 1],
                                            hiA[:, t % 2, 1].bitcast(fp32), ALU.subtract
                                            ).then_inc(loA_ready, 1)
                if t == ONE_FROM - 1:
                    pool.wait_ge(down_summed, DOWN_UNITS)
                    nc.gpsimd.memset(st_full2, 0.0).then_inc(stationaries_zeroed, 1)
                if t == 2:
                    pool.wait_ge(base_u_loaded, 16 * 4)
                if 0 <= t - BU_AT < UP_UNITS:
                    pool.wait_ge(x_turned, 2 * (t - BU_AT + 1))
                    add_bu(t - BU_AT)
            for v in range(UP_UNITS + BU_DVE_UNITS, 2 * UP_UNITS):
                add_bu(v)

        @block.tensor
        def _(pe):
            pe.wait_ge(cond_spread, 1)
            pe.wait_ge(ident_ready, 1)
            for r in range(R):
                last = nc.tensor.transpose(gt[:, 0, r * B:(r + 1) * B],
                                           cond_rep[:, r].rearrange("b q i -> b (q i)"), ident[0:B, 0:B])
            last.then_inc(cond_turned, 1)

            def stationary(st, r, s):
                return st[:, r, s * P:(s + 1) * P]

            def sum_a_full(c, u, a):
                s = u % SLOTS
                pe.wait_ge(tA_ready, c + 1)
                nc.tensor.matmul(a, stationary(st_full, 0, s), tA[:, u % 2, 0], start=s == 0, stop=False)
                nc.tensor.matmul(a, stationary(st_full, 1, s), tA[:, u % 2, 1], start=False, stop=False
                                 ).then_inc(sumA_done, 1)

            def add_split(a, moving, r, s, start=False, stop=False):
                return nc.tensor.matmul(a, stationary(st_split, r, s), moving, start=start, stop=stop)

            def sum_b(c, u, a, stop):
                s = u % SLOTS
                pe.wait_ge(hiB_ready, c + 1)
                add_split(a, hiB[:, u % 2, 0], 2, s)
                add_split(a, hiB[:, u % 2, 1], 3, s)
                pe.wait_ge(loB_ready, c + 1)
                add_split(a, loB[:, u % 2, 0], 2, s)
                add_split(a, loB[:, u % 2, 1], 3, s, stop=stop).then_inc(sumB_done, 1)

            def turn_group(g, n):
                pe.wait_ge(g_ready, g + 1)
                if later(g, 1):
                    pe.wait_ge(group_added, g)
                for k in range(C):
                    last = nc.tensor.transpose(gt[:, k], g_rows[:, n, k * P:(k + 1) * P], ident[:])
                last.then_inc(g_turned, 1)

            pe.wait_ge(full_ready, Q)

            def turn(it):
                for u in range(GROUP_CHUNKS_LOOPED):
                    c, s, n = GROUP_CHUNKS_LOOPED * it + u, u % SLOTS, u // SLOTS
                    if s == 0 and later(it, 1):
                        pe.wait_ge(g_ready, 2 * it + n - 1)
                    sum_a_full(c, u, acc[n][:])
                    if u == 0 and isinstance(it, int):
                        pe.wait_ge(split_ready, 2 * Q)
                    sum_b(c, u, acc[n][:], stop=s == SLOTS - 1)
                    if u == 4 and isinstance(it, int):
                        pe.wait_ge(base_summed, 1)
                        for k in range(C):
                            last = nc.tensor.transpose(bank[0][:, k * P:(k + 1) * P], wd_nat[:, k], ident[:])
                        last.then_inc(base_turned, 1)
                    if u == 1 and not isinstance(it, int):
                        turn_group(2 * it - 1, 1)
                    if u == SLOTS + 1:
                        turn_group(2 * it, 0)

            turn(0)
            with pe.Fori(1, TURNS) as it:
                turn(it)

            def turn_x(m):
                j, c0 = m // 2, m % 2 * BANK_C
                b, i0 = j // BATCH_UNITS, j % BATCH_UNITS * UNIT_I
                pe.wait_ge(x_loaded[(b * I + i0) * X_PIECES // (B * I)], 16)
                if m >= BANK_RING:
                    pe.wait_ge(x_copied, m - BANK_RING + 1)
                for n, (c, i) in enumerate((c, i) for c in range(c0, c0 + BANK_C) for i in range(UNIT_I)):
                    last = nc.tensor.transpose(bank[m % BANK_RING][:, n * P:(n + 1) * P],
                                               xs[:, b, i0 + i, c * P:(c + 1) * P], ident[:])
                last.then_inc(x_turned, 1)

            def down_unit(j):
                pe.wait_ge(group_added, GROUPS)
                pe.wait_ge(x_copied, 2 * (j + 1))
                if j >= 1:
                    pe.wait_ge(down_ready, j)
                for c in range(C):
                    last = nc.tensor.matmul(dn[:], wd_b[:, c, j // BATCH_UNITS], xt[:, j % XT_RING, c],
                                            start=c == 0, stop=c == C - 1)
                last.then_inc(down_summed, 1)

            def up_unit(v):
                half, b, i0 = v // UP_UNITS, v % UP_UNITS // (I // UP_I), v % (I // UP_I) * UP_I
                pe.wait_ge(group_added, GROUPS + (half + 1) * GROUPS // 2)
                pe.wait_ge(down_ready, (b * I + i0 + UP_I) // UNIT_I)
                if v == 0:
                    pe.wait_ge(x_copied, X_BANKS)
                if v >= BANK_RING:
                    pe.wait_ge(unit_final, v - BANK_RING + 1)
                for i in range(UP_I):
                    last = nc.tensor.matmul(bank[v % BANK_RING][:, i * HALF:(i + 1) * HALF],
                                            down[:, b, i0 + i], wu_b[:, b, half * HALF:(half + 1) * HALF],
                                            start=True, stop=True)
                last.then_inc(up_summed, 1)

            for t in range(CHUNKS):
                c, s, n = CHUNKS + t, t % SLOTS, t // SLOTS % 2
                if s == 0:
                    pe.wait_ge(g_ready, c // SLOTS - 1)
                if BOTH_FROM <= t < ONE_FROM:
                    pe.wait_ge(hiA_ready, t - BOTH_FROM + 1)
                    add_split(acc[n][:], hiA[:, t % 2, 0], 0, s, start=s == 0)
                    add_split(acc[n][:], hiA[:, t % 2, 1], 1, s)
                    pe.wait_ge(loA_ready, t - BOTH_FROM + 1)
                    add_split(acc[n][:], loA[:, t % 2, 0], 0, s)
                    add_split(acc[n][:], loA[:, t % 2, 1], 1, s).then_inc(sumA_done, 1)
                elif t < BOTH_FROM:
                    sum_a_full(c, t, acc[n][:])
                else:
                    if t == ONE_FROM:
                        pe.wait_ge(full_ready, 2 * Q)
                    pe.wait_ge(tA_ready, c + 1)
                    nc.tensor.matmul(acc[n][:], stationary(st_full2, 0, s), tA[:, t % 2, 0],
                                     start=s == 0, stop=False)
                if t < X_BANKS // 2:
                    turn_x(2 * t)
                if t in DOWN_AT:
                    down_unit(DOWN_AT[t])
                if t in UP_AT_A:
                    up_unit(UP_AT_A[t])
                if s == 1:
                    g = c // SLOTS - 1
                    if t == SLOTS + 1:
                        pe.wait_ge(base_ready, 2)
                    turn_group(g, g % 2)
                sum_b(c, t, acc[n][:], stop=s == SLOTS - 1 and t < ONE_FROM)
                if t >= ONE_FROM:
                    pe.wait_ge(hiA_ready, t - BOTH_FROM + 1)
                    add_split(acc[n][:], hiA[:, t % 2, 1], 1, s)
                    pe.wait_ge(loA_ready, t - BOTH_FROM + 1)
                    add_split(acc[n][:], loA[:, t % 2, 1], 1, s, stop=s == SLOTS - 1
                              ).then_inc(sumA_done, 1)
                if t < X_BANKS // 2:
                    turn_x(2 * t + 1)
                if t in UP_AT_B:
                    up_unit(UP_AT_B[t])
                if t == SLOTS:
                    pe.wait_ge(base_summed, 2)
                    pe.wait_ge(group_added, GROUPS)
                    for k in range(C):
                        last = nc.tensor.transpose(gt[:, k], wu_nat[:, k], ident[:])
                    last.then_inc(base_turned, 1)
            turn_group(2 * GROUPS - 1, 1)
            for v in range(UP_UNITS, 2 * UP_UNITS):
                up_unit(v)


_INS = ['x', 'cond_256', 'L0_cond_Wd', 'L0_cond_bd', 'L0_cond_Wu', 'L0_cond_bu',
        'L0_cond_Wdd', 'L0_cond_bdd', 'L0_cond_Wdu', 'L0_cond_bdu']
_OUTS = [((B, L, D), 'float32')]


def kernel(**inputs):
    import numpy as _np
    import concourse.bacc as _bacc
    from concourse import mybir as _mybir
    from concourse.bass_utils import run_bass_kernel_spmd as _run

    nc = _bacc.Bacc("TRN2", target_bir_lowering=False, num_devices=1)
    arrays, args = {}, []
    for name in _INS:
        a = _np.ascontiguousarray(inputs[name])
        arrays[f"in_{name}_dram"] = a
        args.append(nc.dram_tensor(f"in_{name}_dram", a.shape, _mybir.dt.from_np(a.dtype), kind="ExternalInput").ap())
    for i, (shape, dtype) in enumerate(_OUTS):
        dt = _mybir.dt.from_np(_np.dtype(dtype))
        args.append(nc.dram_tensor(f"out_{i}_dram", shape, dt, kind="ExternalOutput").ap())
    hyper_adapter(nc, *args)
    r = _run(nc, [arrays], core_ids=[0])
    return r.results[0]["out_0_dram"]
```
